# Optimizing a Trainium2 kernel written in Bass

```python
import numpy as np
import jax
import jax.numpy as jnp

def _softmax(x, axis=-1):
    return jax.nn.softmax(x, axis=axis)

def _gelu(x):
    return jax.nn.gelu(x, approximate=True)

def _silu(x):
    return jax.nn.silu(x)

def _sigmoid(x):
    return jax.nn.sigmoid(x)

def _layernorm(x, axis=-1, eps=1e-05):
    m = jnp.mean(x, axis=axis, keepdims=True)
    v = jnp.var(x, axis=axis, keepdims=True)
    return (x - m) / jnp.sqrt(v + eps)

def _scatter_add(tgt, idx, src, axis=0):
    return tgt.at[idx].add(src)

def _segment_sum(src, seg, n):
    return jax.ops.segment_sum(src, seg, n)
kernel_name = 'mk_sandwich_d2_jaxref_r4_e08bd5'

def setup_inputs(seed: int=0):
    np.random.seed(seed)
    _w = jnp.asarray

    def _L0_attn_setup():
        import jax, jax.numpy as jnp
        import numpy as np
        EPS = 1e-05
        NUM_HEADS = 16

        def _linear_attention(x, Wq, Wk, Wv, Wo, bo):
            B, L, E = x.shape
            H = NUM_HEADS
            D = E // H
            q = (x @ Wq.T).reshape(B, L, H, D)
            k = (x @ Wk.T).reshape(B, L, H, D)
            v = (x @ Wv.T).reshape(B, L, H, D)
            phi_q = jax.nn.elu(q) + 1.0
            phi_k = jax.nn.elu(k) + 1.0
            pq = jnp.moveaxis(phi_q, 1, 0)
            pk = jnp.moveaxis(phi_k, 1, 0)
            vt = jnp.moveaxis(v, 1, 0)
            S0 = jnp.zeros((B, H, D, D), x.dtype)
            z0 = jnp.zeros((B, H, D), x.dtype)

            def step(carry, inp):
                S, z = carry
                pq_t, pk_t, v_t = inp
                S = S + pk_t[..., :, None] * v_t[..., None, :]
                z = z + pk_t
                num = jnp.einsum('bhd,bhde->bhe', pq_t, S)
                den = jnp.sum(pq_t * z, axis=-1, keepdims=True) + EPS
                return ((S, z), num / den)
            (_, _), out = jax.lax.scan(step, (S0, z0), (pq, pk, vt))
            out = jnp.moveaxis(out, 0, 1).reshape(B, L, E)
            return out @ Wo.T + bo
        key = jax.random.key(seed)
        ks = jax.random.split(key, 6)
        B, L, E = (4, 1024, 256)
        s = 1.0 / np.sqrt(E)
        return {'x': jax.random.normal(ks[0], (B, L, E), jnp.float32), 'Wq': jax.random.normal(ks[1], (E, E), jnp.float32) * s, 'Wk': jax.random.normal(ks[2], (E, E), jnp.float32) * s, 'Wv': jax.random.normal(ks[3], (E, E), jnp.float32) * s, 'Wo': jax.random.normal(ks[4], (E, E), jnp.float32) * s, 'bo': jnp.zeros((E,), jnp.float32)}
    _L0_attn_in = _L0_attn_setup()

    def _L0_ffn_setup():
        import jax, jax.numpy as jnp
        import numpy as np
        DIM = 256
        HIDDEN = 768
        SCALE = 1.0 / 127.0

        def _dequant(w_int, dtype):
            return w_int.astype(dtype) * jnp.asarray(SCALE, dtype)
        key = jax.random.key(seed)
        k_x, k_g, k_u, k_d = jax.random.split(key, 4)
        x = jax.random.normal(k_x, (4, 512, DIM), dtype=jnp.float32)
        w_gate = jax.random.randint(k_g, (HIDDEN, DIM), -127, 128, dtype=jnp.int32)
        w_up = jax.random.randint(k_u, (HIDDEN, DIM), -127, 128, dtype=jnp.int32)
        w_down = jax.random.randint(k_d, (DIM, HIDDEN), -127, 128, dtype=jnp.int32)
        return {'x': x, 'w_gate': w_gate, 'w_up': w_up, 'w_down': w_down}
    _L0_ffn_in = _L0_ffn_setup()

    def _L1_attn_setup():
        import jax, jax.numpy as jnp
        import numpy as np
        HID = 256
        NH = 16
        HD = HID // NH
        RD = int(HD * 0.25)
        B = 2
        S = 512
        ROPE_BASE = 10000.0

        def _rotary_tables(seq_len):
            inv_freq = 1.0 / ROPE_BASE ** (jnp.arange(0, RD, 2, dtype=jnp.float32) / RD)
            t = jnp.arange(seq_len, dtype=jnp.float32)
            freqs = jnp.outer(t, inv_freq)
            emb = jnp.concatenate([freqs, freqs], axis=-1)
            return (jnp.cos(emb)[None, None], jnp.sin(emb)[None, None])

        def _rotate_half(x):
            x1, x2 = jnp.split(x, 2, axis=-1)
            return jnp.concatenate([-x2, x1], axis=-1)
        key = jax.random.key(seed)
        ks = jax.random.split(key, 4)
        hidden_states = jax.random.normal(ks[0], (B, S, HID), jnp.float32)
        Wqkv = jax.random.normal(ks[1], (3 * HID, HID), jnp.float32) * HID ** (-0.5)
        bqkv = jnp.zeros((3 * HID,), jnp.float32)
        Wd = jax.random.normal(ks[2], (HID, HID), jnp.float32) * HID ** (-0.5)
        bd = jnp.zeros((HID,), jnp.float32)
        return {'hidden_states': hidden_states, 'Wqkv': Wqkv, 'bqkv': bqkv, 'Wd': Wd, 'bd': bd}
    _L1_attn_in = _L1_attn_setup()

    def _L1_ffn_setup():
        import jax, jax.numpy as jnp
        import numpy as np
        D = 256
        F = 256
        E = 8
        K = 2
        B, T = (2, 512)

        def _moe_forward(x, router_w, w1, w2, shared_gate_up, shared_down, shared_gate_w):
            b, t, d = x.shape
            xf = x.reshape(-1, d)
            n = xf.shape[0]
            logits = xf @ router_w
            probs = jax.nn.softmax(logits, axis=-1)
            topw, topi = jax.lax.top_k(probs, K)
            combine = jnp.zeros((n, E), dtype=probs.dtype).at[jnp.arange(n)[:, None], topi].add(topw)
            h = jax.nn.silu(jnp.einsum('nd,edf->nef', xf, w1))
            ye = jnp.einsum('nef,efd->ned', h, w2)
            routed = jnp.einsum('ne,ned->nd', combine, ye)
            gu = xf @ shared_gate_up
            gate, up = (gu[:, :F], gu[:, F:])
            shared = jax.nn.silu(gate) * up @ shared_down
            shared = jax.nn.sigmoid(xf @ shared_gate_w) * shared
            return (routed + shared).reshape(b, t, d)
        key = jax.random.key(seed)
        ks = jax.random.split(key, 7)
        std = 0.02
        x = jax.random.normal(ks[0], (B, T, D), dtype=jnp.float32)
        router_w = jax.random.normal(ks[1], (D, E), dtype=jnp.float32) * std
        w1 = jax.random.normal(ks[2], (E, D, F), dtype=jnp.float32) * std
        w2 = jax.random.normal(ks[3], (E, F, D), dtype=jnp.float32) * std
        shared_gate_up = jax.random.normal(ks[4], (D, 2 * F), dtype=jnp.float32) * std
        shared_down = jax.random.normal(ks[5], (F, D), dtype=jnp.float32) * std
        shared_gate_w = jax.random.normal(ks[6], (D, 1), dtype=jnp.float32) * std
        return {'x': x, 'router_w': router_w, 'w1': w1, 'w2': w2, 'shared_gate_up': shared_gate_up, 'shared_down': shared_down, 'shared_gate_w': shared_gate_w}
    _L1_ffn_in = _L1_ffn_setup()
    _d = {'L0_attn_x': _L0_attn_in['x'], 'L0_attn_Wq': _L0_attn_in['Wq'], 'L0_attn_Wk': _L0_attn_in['Wk'], 'L0_attn_Wv': _L0_attn_in['Wv'], 'L0_attn_Wo': _L0_attn_in['Wo'], 'L0_attn_bo': _L0_attn_in['bo'], 'L0_ffn_w_gate': _L0_ffn_in['w_gate'], 'L0_ffn_w_up': _L0_ffn_in['w_up'], 'L0_ffn_w_down': _L0_ffn_in['w_down'], 'L1_attn_Wqkv': _L1_attn_in['Wqkv'], 'L1_attn_bqkv': _L1_attn_in['bqkv'], 'L1_attn_Wd': _L1_attn_in['Wd'], 'L1_attn_bd': _L1_attn_in['bd'], 'L1_ffn_router_w': _L1_ffn_in['router_w'], 'L1_ffn_w1': _L1_ffn_in['w1'], 'L1_ffn_w2': _L1_ffn_in['w2'], 'L1_ffn_shared_gate_up': _L1_ffn_in['shared_gate_up'], 'L1_ffn_shared_down': _L1_ffn_in['shared_down'], 'L1_ffn_shared_gate_w': _L1_ffn_in['shared_gate_w']}
    _x0 = _d['L0_attn_x']
    _d['L0_attn_x'] = jax.random.normal(jax.random.fold_in(jax.random.key(seed), 1), (4, 1024, 256), dtype=_x0.dtype)
    del _x0
    return _d

def reference(L0_attn_x, L0_attn_Wq, L0_attn_Wk, L0_attn_Wv, L0_attn_Wo, L0_attn_bo, L0_ffn_w_gate, L0_ffn_w_up, L0_ffn_w_down, L1_attn_Wqkv, L1_attn_bqkv, L1_attn_Wd, L1_attn_bd, L1_ffn_router_w, L1_ffn_w1, L1_ffn_w2, L1_ffn_shared_gate_up, L1_ffn_shared_down, L1_ffn_shared_gate_w):

    def _L0_attn_ref(x, Wq, Wk, Wv, Wo, bo):
        import jax, jax.numpy as jnp
        import numpy as np
        EPS = 1e-05
        NUM_HEADS = 16

        def _linear_attention(x, Wq, Wk, Wv, Wo, bo):
            B, L, E = x.shape
            H = NUM_HEADS
            D = E // H
            q = (x @ Wq.T).reshape(B, L, H, D)
            k = (x @ Wk.T).reshape(B, L, H, D)
            v = (x @ Wv.T).reshape(B, L, H, D)
            phi_q = jax.nn.elu(q) + 1.0
            phi_k = jax.nn.elu(k) + 1.0
            pq = jnp.moveaxis(phi_q, 1, 0)
            pk = jnp.moveaxis(phi_k, 1, 0)
            vt = jnp.moveaxis(v, 1, 0)
            S0 = jnp.zeros((B, H, D, D), x.dtype)
            z0 = jnp.zeros((B, H, D), x.dtype)

            def step(carry, inp):
                S, z = carry
                pq_t, pk_t, v_t = inp
                S = S + pk_t[..., :, None] * v_t[..., None, :]
                z = z + pk_t
                num = jnp.einsum('bhd,bhde->bhe', pq_t, S)
                den = jnp.sum(pq_t * z, axis=-1, keepdims=True) + EPS
                return ((S, z), num / den)
            (_, _), out = jax.lax.scan(step, (S0, z0), (pq, pk, vt))
            out = jnp.moveaxis(out, 0, 1).reshape(B, L, E)
            return out @ Wo.T + bo
        return _linear_attention(x, Wq, Wk, Wv, Wo, bo)

    def _L0_ffn_ref(x, w_gate, w_up, w_down):
        import jax, jax.numpy as jnp
        import numpy as np
        DIM = 256
        HIDDEN = 768
        SCALE = 1.0 / 127.0

        def _dequant(w_int, dtype):
            return w_int.astype(dtype) * jnp.asarray(SCALE, dtype)
        wg = _dequant(w_gate, x.dtype)
        wu = _dequant(w_up, x.dtype)
        wd = _dequant(w_down, x.dtype)
        gate = jnp.einsum('bsd,hd->bsh', x, wg)
        up = jnp.einsum('bsd,hd->bsh', x, wu)
        h = jax.nn.silu(gate) * up
        return jnp.einsum('bsh,dh->bsd', h, wd)

    def _L1_attn_ref(hidden_states, Wqkv, bqkv, Wd, bd):
        import jax, jax.numpy as jnp
        import numpy as np
        HID = 256
        NH = 16
        HD = HID // NH
        RD = int(HD * 0.25)
        B = 2
        S = 512
        ROPE_BASE = 10000.0

        def _rotary_tables(seq_len):
            inv_freq = 1.0 / ROPE_BASE ** (jnp.arange(0, RD, 2, dtype=jnp.float32) / RD)
            t = jnp.arange(seq_len, dtype=jnp.float32)
            freqs = jnp.outer(t, inv_freq)
            emb = jnp.concatenate([freqs, freqs], axis=-1)
            return (jnp.cos(emb)[None, None], jnp.sin(emb)[None, None])

        def _rotate_half(x):
            x1, x2 = jnp.split(x, 2, axis=-1)
            return jnp.concatenate([-x2, x1], axis=-1)
        b, s, _ = hidden_states.shape
        qkv = hidden_states @ Wqkv.T + bqkv
        qkv = qkv.reshape(b, s, 3, NH, HD).transpose(2, 0, 3, 1, 4)
        q, k, v = (qkv[0], qkv[1], qkv[2])
        cos, sin = _rotary_tables(s)
        q_rot, q_pass = (q[..., :RD], q[..., RD:])
        k_rot, k_pass = (k[..., :RD], k[..., RD:])
        q_rot = q_rot * cos + _rotate_half(q_rot) * sin
        k_rot = k_rot * cos + _rotate_half(k_rot) * sin
        q = jnp.concatenate([q_rot, q_pass], axis=-1)
        k = jnp.concatenate([k_rot, k_pass], axis=-1)
        scale = HD ** (-0.5)
        logits = jnp.einsum('bhqd,bhkd->bhqk', q, k) * scale
        causal_mask = jnp.triu(jnp.full((s, s), -jnp.inf, dtype=logits.dtype), 1)
        probs = jax.nn.softmax(logits + causal_mask, axis=-1)
        L = jnp.eye(s, dtype=probs.dtype) - jnp.tril(probs, -1)
        rhs = jnp.diagonal(probs, axis1=-2, axis2=-1)[..., None] * v
        A = jax.scipy.linalg.solve_triangular(L, rhs, lower=True)
        attn_output = A.transpose(0, 2, 1, 3).reshape(b, s, HID)
        return attn_output @ Wd.T + bd

    def _L1_ffn_ref(x, router_w, w1, w2, shared_gate_up, shared_down, shared_gate_w):
        import jax, jax.numpy as jnp
        import numpy as np
        D = 256
        F = 256
        E = 8
        K = 2
        B, T = (2, 512)

        def _moe_forward(x, router_w, w1, w2, shared_gate_up, shared_down, shared_gate_w):
            b, t, d = x.shape
            xf = x.reshape(-1, d)
            n = xf.shape[0]
            logits = xf @ router_w
            probs = jax.nn.softmax(logits, axis=-1)
            topw, topi = jax.lax.top_k(probs, K)
            combine = jnp.zeros((n, E), dtype=probs.dtype).at[jnp.arange(n)[:, None], topi].add(topw)
            h = jax.nn.silu(jnp.einsum('nd,edf->nef', xf, w1))
            ye = jnp.einsum('nef,efd->ned', h, w2)
            routed = jnp.einsum('ne,ned->nd', combine, ye)
            gu = xf @ shared_gate_up
            gate, up = (gu[:, :F], gu[:, F:])
            shared = jax.nn.silu(gate) * up @ shared_down
            shared = jax.nn.sigmoid(xf @ shared_gate_w) * shared
            return (routed + shared).reshape(b, t, d)
        return _moe_forward(x, router_w, w1, w2, shared_gate_up, shared_down, shared_gate_w)
    x = L0_attn_x
    x = x + _layernorm(_L0_attn_ref(_layernorm(x, axis=-1), L0_attn_Wq, L0_attn_Wk, L0_attn_Wv, L0_attn_Wo, L0_attn_bo), axis=-1)
    x = x + _layernorm(_L0_ffn_ref(_layernorm(x, axis=-1), L0_ffn_w_gate, L0_ffn_w_up, L0_ffn_w_down), axis=-1)
    x = x + _layernorm(_L1_attn_ref(_layernorm(x, axis=-1), L1_attn_Wqkv, L1_attn_bqkv, L1_attn_Wd, L1_attn_bd), axis=-1)
    x = x + _layernorm(_L1_ffn_ref(_layernorm(x, axis=-1), L1_ffn_router_w, L1_ffn_w1, L1_ffn_w2, L1_ffn_shared_gate_up, L1_ffn_shared_down, L1_ffn_shared_gate_w), axis=-1)
    return x

_drawn_inputs = setup_inputs


def setup_inputs(seed=0):
    import zlib

    import numpy as np

    out = dict(_drawn_inputs(seed))
    spreads = {'L0_attn_bo': (0.0, 0.1), 'L1_attn_bqkv': (0.0, 0.1), 'L1_attn_bd': (0.0, 0.1)}
    factors = {}
    for name, (base, spread) in spreads.items():
        noise = np.random.default_rng([zlib.crc32(name.encode()), seed]).standard_normal(out[name].shape)
        drawn = base * np.exp(spread * noise) if base else spread * noise
        out[name] = jnp.asarray(drawn.astype(out[name].dtype))
    for name, factor in factors.items():
        out[name] = (out[name] * factor).astype(out[name].dtype)
    return out
```

```python
from contextlib import ExitStack

import numpy as np

import concourse.bass as bass
from concourse import mybir

F32 = mybir.dt.float32
BF16 = mybir.dt.bfloat16
I32 = mybir.dt.int32
ALU = mybir.AluOpType
ACT = mybir.ActivationFunctionType
AX = mybir.AxisListType.X

P = 128
C = 256
KC = C // P
BATCH, SEQ = 4, 1024
TILES = BATCH * SEQ // P
TPB = SEQ // P
NH, HD = 16, 16
OCT = NH * HD // P
HPO = NH // OCT
VW = HD + 1
GT = 4
GROUPS = TILES // GT
GW = GT * P
HID = 768
MC = HID // P
SCALE = 1.0 / 127.0
EPS = 1e-5


def scope(nc, ctx, prefix):
    def sb(name, shape, dt=F32):
        return ctx.enter_context(nc.sbuf_tensor(f"{prefix}_{name}", shape, dt))

    def ps(name, shape, dt=F32):
        return ctx.enter_context(nc.psum_tensor(f"{prefix}_{name}", shape, dt))

    def sem(name):
        return ctx.enter_context(nc.semaphore(f"{prefix}_{name}"))

    return sb, ps, sem


def hold(eng, sem, value, passed):
    eng.wait_ge(sem, value)
    if not isinstance(value, int):
        eng.sem_inc(passed, 1)


def constants_of_shapes():
    p = np.arange(P)
    eye = np.eye(P, dtype=np.float32)
    causal_t = (p[:, None] <= p[None, :]).astype(np.float32)
    causal_bias = np.where(p[None, :] > p[:, None], -1e30, 0.0).astype(np.float32)
    parity = np.stack([(p // HD) % 2 == 0, (p // HD) % 2 == 1], 1).astype(np.float32)
    block = np.repeat((p[:, None] // HD == np.arange(HPO)[None, :]).astype(np.float32), VW, axis=1)
    rd = HD // 4
    inv = 1.0 / 10000.0 ** (np.arange(0, rd, 2, dtype=np.float32) / rd)
    ang = np.outer(np.arange(SEQ, dtype=np.float32), inv).astype(np.float32)
    cos = np.concatenate([np.cos(ang), np.cos(ang)], 1)
    sin = np.concatenate([-np.sin(ang), np.sin(ang)], 1)
    def tiles(a):
        return a.reshape(TPB, P, rd).transpose(1, 0, 2).reshape(P, TPB * rd)

    before = np.tile((np.arange(8)[None, :] < np.arange(8)[:, None]).astype(np.float32).reshape(1, 64), (P, 1))
    parts = dict(eye=eye, causal_t=causal_t, causal_bias=causal_bias, parity=parity, block=block,
                 cos=tiles(cos), sin=tiles(sin), before=before,
                 neg_half=np.full((P, GT), -0.5, np.float32))
    at, spans = 0, {}
    for k, v in parts.items():
        spans[k] = (at, at + v.shape[1])
        at += v.shape[1]
    return np.concatenate(list(parts.values()), 1).astype(np.float32), spans


def linear_attention_layer(nc, x_sb, const, wq, wk, wv, wo, bo, x_dram):
    with ExitStack() as ctx:
        sb, ps, sem = scope(nc, ctx, "lin")
        w_qkv = sb("w_qkv", [P, KC, 3 * C])
        w_o = sb("w_o", [P, KC, C])
        b_o = sb("b_o", [P, C])
        x_norm = sb("x_norm", [P, C])
        xT = sb("xT", [P, 2, KC, P])
        clipped = sb("clipped", [P, 2 * C])
        grown = sb("grown", [P, 2 * C])
        phi = sb("phi", [P, 2, 2 * C])
        phiT = sb("phiT", [P, 2, 4, P])
        q_par = sb("q_par", [P, 2, OCT, 2, P])
        v_ones = sb("v_ones", [P, 2, NH * VW])
        scores = sb("scores", [P, 4, OCT, 2, P])
        state = sb("state", [P, OCT * HPO * VW])
        state_new = sb("state_new", [P, OCT * HPO * VW])
        den = sb("den", [P, NH])
        attn = sb("attn", [P, C])
        attnT = sb("attnT", [P, KC, P])
        y = sb("y", [P, C])
        z = sb("z", [P, C])
        st_in, st_out = sb("st_in", [P, 6]), sb("st_out", [P, 6])
        mv_in, mv_out = sb("mv_in", [P, 2]), sb("mv_out", [P, 2])
        ve_in, ve_out = sb("ve_in", [P, 1]), sb("ve_out", [P, 1])
        rs_in, rs_out = sb("rs_in", [P, 1]), sb("rs_out", [P, 1])
        neg_half = sb("neg_half", [P, 1])
        ps_T = ps("ps_T", [P, 512])
        ps_qk = ps("ps_qk", [P, 512])
        ps_v = ps("ps_v", [P, 512])
        ps_out = ps("ps_out", [P, 512])
        ps_s = ps("ps_s", [P, 4, OCT, 2, P])
        ps_state = ps_s[:, 0].rearrange("p a b c -> p (a b c)")

        m = {n: sem(n) for n in (
            "x_loaded", "x_rest_loaded", "w_loaded", "ones_set", "stats_in", "aggr_in", "var_in", "rstd_in", "normed", "x_turned",
            "xT_ready", "qk_projected", "v_projected", "v_copied", "qk_clipped", "qk_grown", "phi_ready",
            "phi_turned", "phiT_ready", "scored", "masked", "state_done", "state_masked", "state_added",
            "out_done", "den_eps", "den_rec", "attn_ready", "attn_turned", "attnT_ready", "y_projected", "y_biased",
            "stats_out", "aggr_out", "var_out", "rstd_out", "y_normed", "x_added")}
        eye, causal, parity, block = const["eye"], const["causal_t"], const["parity"], const["block"]

        with nc.Block() as blk:
            @blk.sync
            def _(sp):
                sp.dma_start(const["all"], const["dram"]).then_inc(m["x_loaded"], 16)

                def load_x(b, loaded):
                    sp.dma_start(x_sb[:, b * TPB:(b + 1) * TPB, :],
                                 x_dram[b].rearrange("(t p) c -> p t c", p=P)).then_inc(loaded, 16)

                load_x(0, m["x_loaded"])
                for n, w in enumerate((wq, wk, wv)):
                    sp.dma_start(w_qkv[:, :, n * C:(n + 1) * C],
                                 w.rearrange("(k p) n -> p k n", p=P)).then_inc(m["w_loaded"], 16)
                sp.dma_start(w_o[:], wo.rearrange("(k p) n -> p k n", p=P)).then_inc(m["w_loaded"], 16)
                sp.dma_start(b_o[:], bo).then_inc(m["w_loaded"], 16)
                for b in range(1, BATCH):
                    load_x(b, m["x_rest_loaded"])

            @blk.gpsimd
            def _(pool):
                pool.memset(neg_half[:], -0.5).then_inc(m["ones_set"], 1)
                pool.memset(v_ones[:], 1.0).then_inc(m["ones_set"], 1)
                pool.memset(state[:], 0.0).then_inc(m["ones_set"], 1)
                pool.wait_ge(m["ones_set"], 3)

                def rstd_of_x(t):
                    pool.wait_ge(m["var_in"], t + 1)
                    pool.tensor_tensor(rs_in[:], ve_in[:], neg_half[:], ALU.pow).then_inc(m["rstd_in"], 1)

                def finish(t):
                    pool.wait_ge(m["var_out"], t + 1)
                    pool.tensor_tensor(rs_out[:], ve_out[:], neg_half[:], ALU.pow).then_inc(m["rstd_out"], 1)
                    pool.wait_ge(m["y_normed"], t + 1)
                    pool.tensor_tensor(x_sb[:, t, :], x_sb[:, t, :], z[:], ALU.add).then_inc(m["x_added"], 1)

                for t in range(3):
                    rstd_of_x(t)
                with pool.Fori(0, TILES - 3) as t:
                    rstd_of_x(t + 3)
                    finish(t)
                for t in range(TILES - 3, TILES):
                    finish(t)

            @blk.vector
            def _(dve):
                def stats(t):
                    dve.bn_stats(st_in[:], x_sb[:, t, :]).then_inc(m["stats_in"], 1)
                    hold(dve, m["stats_in"], t + 1, const["passed"])
                    dve.bn_aggr(mv_in[:], st_in[:]).then_inc(m["aggr_in"], 1)
                    dve.wait_ge(m["aggr_in"], t + 1)
                    dve.tensor_scalar(ve_in[:], mv_in[:, 1:2], EPS, None, ALU.add).then_inc(m["var_in"], 1)

                def norm(t):
                    dve.wait_ge(m["rstd_in"], t + 1)
                    dve.tensor_scalar(x_norm[:], x_sb[:, t, :], mv_in[:, 0:1], rs_in[:, 0:1],
                                      ALU.subtract, ALU.mult).then_inc(m["normed"], 1)

                def clip(t):
                    dve.wait_ge(m["qk_projected"], t + 1)
                    dve.tensor_scalar(clipped[:], ps_qk[:], 0.0, None, ALU.min).then_inc(m["qk_clipped"], 1)

                def features(t, b):
                    dve.wait_ge(m["qk_grown"], t + 1)
                    dve.scalar_tensor_tensor(phi[:, b], ps_qk[:], 0.0, grown[:], ALU.max,
                                             ALU.add).then_inc(m["phi_ready"], 1)

                def mask(t):
                    for h in range(2):
                        dve.wait_ge(m["scored"], 2 * t + h + 1)
                        v = scores[:, 2 * h:2 * h + 2].rearrange("p a b c q -> p (a b c) q")
                        dve.tensor_tensor(v, ps_s[:, 2 * h:2 * h + 2].rearrange("p a b c q -> p (a b c) q"),
                                          causal.unsqueeze(1).broadcast_to([P, 2 * OCT * 2, P]), ALU.mult
                                          ).then_inc(m["masked"], 1)

                def attend(t, b):
                    n = OCT * HPO * VW
                    dve.wait_ge(m["state_done"], t + 1)
                    dve.tensor_tensor(state_new[:].rearrange("p (o j) -> p o j", o=OCT),
                                      ps_state[:, 0:n].rearrange("p (o j) -> p o j", o=OCT),
                                      block.unsqueeze(1).broadcast_to([P, OCT, HPO * VW]),
                                      ALU.mult).then_inc(m["state_masked"], 1)
                    dve.wait_ge(m["out_done"], t + 1)
                    o = ps_out[:, 0:n].rearrange("p (h j) -> p h j", j=VW)
                    dve.tensor_scalar(den[:], o[:, :, HD], EPS, None, ALU.add).then_inc(m["den_eps"], 1)
                    dve.wait_ge(m["den_eps"], t + 1)
                    dve.reciprocal(den[:], den[:]).then_inc(m["den_rec"], 1)
                    dve.wait_ge(m["state_masked"], t + 1)
                    if b is not None:
                        dve.tensor_tensor(state[:], state[:], state_new[:], ALU.add).then_inc(m["state_added"], 1)
                    else:
                        dve.memset(state[:], 0.0).then_inc(m["state_added"], 1)
                    dve.wait_ge(m["den_rec"], t + 1)
                    dve.tensor_tensor(attn[:].rearrange("p (h j) -> p h j", j=HD), o[:, :, 0:HD],
                                      den[:].unsqueeze(2).broadcast_to([P, NH, HD]), ALU.mult
                                      ).then_inc(m["attn_ready"], 1)

                def finish(t):
                    dve.wait_ge(m["y_projected"], t + 1)
                    dve.tensor_tensor(y[:], ps_v[:, C:2 * C], b_o[:], ALU.add).then_inc(m["y_biased"], 1)
                    dve.wait_ge(m["y_biased"], t + 1)
                    dve.bn_stats(st_out[:], y[:]).then_inc(m["stats_out"], 1)
                    hold(dve, m["stats_out"], t + 1, const["passed"])
                    dve.bn_aggr(mv_out[:], st_out[:]).then_inc(m["aggr_out"], 1)
                    dve.wait_ge(m["aggr_out"], t + 1)
                    dve.tensor_scalar(ve_out[:], mv_out[:, 1:2], EPS, None, ALU.add).then_inc(m["var_out"], 1)
                    dve.wait_ge(m["rstd_out"], t + 1)
                    dve.tensor_scalar(z[:], y[:], mv_out[:, 0:1], rs_out[:, 0:1],
                                      ALU.subtract, ALU.mult).then_inc(m["y_normed"], 1)

                def step(t, b, end, left=3):
                    if left > 0:
                        clip(t + 1)
                    mask(t)
                    if left > 1:
                        norm(t + 2)
                    if left > 0:
                        features(t + 1, 1 - b)
                    attend(t, None if end else b)
                    if left > 2:
                        stats(t + 3)
                    finish(t)

                dve.wait_ge(m["x_loaded"], 32)
                dve.wait_ge(m["ones_set"], 3)
                stats(0)
                norm(0)
                stats(1)
                dve.wait_ge(m["x_turned"], 1)
                norm(1)
                clip(0)
                features(0, 0)
                stats(2)
                dve.wait_ge(m["w_loaded"], 16 * 5)
                dve.wait_ge(m["x_rest_loaded"], 16 * (BATCH - 1))
                with dve.Fori(0, BATCH - 1) as row:
                    for c in range(TPB):
                        step(row * TPB + c, c % 2, c == TPB - 1)
                for c in range(TPB):
                    step((BATCH - 1) * TPB + c, c % 2, c == TPB - 1, min(3, TPB - 1 - c))

            @blk.scalar
            def _(act):
                def input_turned(t, b):
                    act.wait_ge(m["x_turned"], t + 1)
                    act.copy(xT[:, b].rearrange("p k t -> p (k t)"), ps_T[:, 0:KC * P]).then_inc(m["xT_ready"], 1)

                def values(t, b):
                    act.wait_ge(m["v_projected"], t + 1)
                    act.copy(v_ones[:, b].rearrange("p (h j) -> p h j", j=VW)[:, :, 0:HD],
                             ps_v[:, 0:C].rearrange("p (h j) -> p h j", j=HD)).then_inc(m["v_copied"], 1)

                def exponential(t):
                    act.wait_ge(m["qk_clipped"], t + 1)
                    act.activation(grown[:], clipped[:], ACT.Exp).then_inc(m["qk_grown"], 1)

                def features_turned(t, b):
                    act.wait_ge(m["phi_turned"], t + 1)
                    act.copy(phiT[:, b].rearrange("p k t -> p (k t)"), ps_qk[:])
                    for e in range(2):
                        last = act.mul(q_par[:, b, :, e, :], ps_qk[:, 0:OCT * P].rearrange("p (o t) -> p o t", o=OCT),
                                       parity[:, e:e + 1])
                    last.then_inc(m["phiT_ready"], 1)

                def attn_turned(t):
                    act.wait_ge(m["attn_turned"], t + 1)
                    act.copy(attnT[:].rearrange("p k t -> p (k t)"), ps_T[:, KC * P:2 * KC * P]
                             ).then_inc(m["attnT_ready"], 1)

                def step(t, b, left=2):
                    if left > 0:
                        exponential(t + 1)
                        values(t + 1, 1 - b)
                    if left > 1:
                        input_turned(t + 2, b)
                    if left > 0:
                        features_turned(t + 1, 1 - b)
                    attn_turned(t)

                act.wait_ge(m["ones_set"], 3)
                input_turned(0, 0)
                input_turned(1, 1)
                exponential(0)
                values(0, 0)
                features_turned(0, 0)
                with act.Fori(0, TILES // 2 - 1) as i:
                    for b in range(2):
                        step(2 * i + b, b)
                step(TILES - 2, 0, 1)
                step(TILES - 1, 1, 0)

            @blk.tensor
            def _(pe):
                def turn_x(t):
                    pe.wait_ge(m["normed"], t + 1)
                    if not (isinstance(t, int) and t < 3):
                        pe.wait_ge(m["attnT_ready"], t - 2)
                    elif t == 1:
                        pe.wait_ge(m["xT_ready"], 1)
                    for k in range(KC):
                        last = pe.transpose(ps_T[:, k * P:(k + 1) * P], x_norm[:, k * P:(k + 1) * P], eye)
                    last.then_inc(m["x_turned"], 1)

                def project(t, b):
                    pe.wait_ge(m["xT_ready"], t + 1)
                    for k in range(KC):
                        last = pe.matmul(ps_qk[:], xT[:, b, k, :], w_qkv[:, k, 0:2 * C],
                                         start=(k == 0), stop=(k == KC - 1))
                    last.then_inc(m["qk_projected"], 1)

                def project_v(t, b):
                    if not (isinstance(t, int) and t < 2):
                        pe.wait_ge(m["y_biased"], t - 1)
                    for k in range(KC):
                        last = pe.matmul(ps_v[:, 0:C], xT[:, b, k, :], w_qkv[:, k, 2 * C:3 * C],
                                         start=(k == 0), stop=(k == KC - 1))
                    last.then_inc(m["v_projected"], 1)

                def turn_phi(t, b):
                    pe.wait_ge(m["phi_ready"], t + 1)
                    for k in range(4):
                        last = pe.transpose(ps_qk[:, k * P:(k + 1) * P], phi[:, b, k * P:(k + 1) * P], eye)
                    last.then_inc(m["phi_turned"], 1)

                def score(t, b):
                    pe.wait_ge(m["phiT_ready"], t + 1)
                    for r in range(4):
                        q = slice(32 * r, 32 * r + 32)
                        for o in range(OCT):
                            last = pe.matmul(ps_s[:, r, o].rearrange("p e t -> p (e t)"), phiT[q, b, OCT + o, :],
                                             q_par[q, b, o].rearrange("p e t -> p (e t)"), start=True, stop=True)
                        if r % 2:
                            last.then_inc(m["scored"], 1)

                def attend(t, b):
                    pe.wait_ge(m["masked"], 2 * t + 1)
                    pe.wait_ge(m["v_copied"], t + 1)
                    w = HPO * VW
                    for o in range(OCT):
                        last = pe.matmul(ps_state[:, o * w:(o + 1) * w], phi[:, b, C + o * P:C + (o + 1) * P],
                                         v_ones[:, b, o * w:(o + 1) * w], start=True, stop=True)
                    last.then_inc(m["state_done"], 1)
                    if not (isinstance(t, int) and t == 0):
                        pe.wait_ge(m["state_added"], t)
                    for o in range(OCT):
                        pe.matmul(ps_out[:, o * w:(o + 1) * w], phiT[:, b, o, :], state[:, o * w:(o + 1) * w],
                                  start=True, stop=False)
                        for h in range(HPO):
                            if (o, h) == (0, HPO // 2):
                                pe.wait_ge(m["masked"], 2 * t + 2)
                            at = (o * HPO + h) * VW
                            last = pe.matmul(ps_out[:, at:at + VW], scores[:, h // 2, o, h % 2, :],
                                             v_ones[:, b, at:at + VW], start=False, stop=(h == HPO - 1))
                    last.then_inc(m["out_done"], 1)

                def turn_attn(t):
                    pe.wait_ge(m["attn_ready"], t + 1)
                    if not (isinstance(t, int) and t > TILES - 3):
                        pe.wait_ge(m["xT_ready"], t + 3)
                    for k in range(KC):
                        last = pe.transpose(ps_T[:, (KC + k) * P:(KC + k + 1) * P], attn[:, k * P:(k + 1) * P], eye)
                    last.then_inc(m["attn_turned"], 1)

                def project_out(t):
                    pe.wait_ge(m["attnT_ready"], t + 1)
                    if not (isinstance(t, int) and t > TILES - 2):
                        pe.wait_ge(m["v_copied"], t + 2)
                    for k in range(KC):
                        last = pe.matmul(ps_v[:, C:2 * C], attnT[:, k, :], w_o[:, k, :],
                                         start=(k == 0), stop=(k == KC - 1))
                    last.then_inc(m["y_projected"], 1)

                def step(t, b, left=2):
                    if left > 0:
                        pe.wait_ge(m["phiT_ready"], t + 1)
                        project(t + 1, 1 - b)
                    score(t, b)
                    if left > 0:
                        project_v(t + 1, 1 - b)
                    if left > 1:
                        turn_x(t + 2)
                    attend(t, b)
                    if left > 0:
                        turn_phi(t + 1, 1 - b)
                    turn_attn(t)
                    project_out(t)

                pe.wait_ge(m["w_loaded"], 16 * 5)
                turn_x(0)
                turn_x(1)
                project(0, 0)
                project_v(0, 0)
                turn_phi(0, 0)
                step(0, 0)
                with pe.Fori(0, TILES // 2 - 2) as i:
                    for k in range(2):
                        step(2 * i + 1 + k, (1 + k) % 2)
                step(TILES - 3, 1)
                step(TILES - 2, 0, 1)
                step(TILES - 1, 1, 0)


def run_steps(eng, n, step):
    step(0, 0, True, False)
    with eng.Fori(0, (n - 2) // 2) as i:
        for j in range(2):
            step(2 * i + 1 + j, (1 + j) % 2, False, False)
    step(n - 1, (n - 1) % 2, False, True)


def group_norm(sb, sem, name, eps, const):
    return dict(eps=eps, passed=const["passed"], neg_half=const["neg_half"],
                stats=sb(name + "_stats", [P, GT, 6]), mv=sb(name + "_mv", [P, GT, 2]),
                var=sb(name + "_var", [P, GT]), rstd=sb(name + "_rstd", [P, GT]),
                stats_done=sem(name + "_stats_done"), aggr_done=sem(name + "_aggr_done"),
                var_done=sem(name + "_var_done"), rstd_done=sem(name + "_rstd_done"))


def norm_measure(ln, dve, tile_of, g):
    for i in range(GT):
        last = dve.bn_stats(ln["stats"][:, i, :], tile_of(i))
    last.then_inc(ln["stats_done"], 1)
    hold(dve, ln["stats_done"], g + 1, ln["passed"])
    for i in range(GT):
        last = dve.bn_aggr(ln["mv"][:, i, :], ln["stats"][:, i, :])
    last.then_inc(ln["aggr_done"], 1)
    dve.wait_ge(ln["aggr_done"], g + 1)
    dve.tensor_scalar(ln["var"][:], ln["mv"][:, :, 1], ln["eps"], None, ALU.add).then_inc(ln["var_done"], 1)


def norm_power(ln, pool, g):
    pool.wait_ge(ln["var_done"], g + 1)
    pool.tensor_tensor(ln["rstd"][:], ln["var"][:], ln["neg_half"], ALU.pow).then_inc(ln["rstd_done"], 1)


def norm_apply(ln, dve, out_of, tile_of, g, done):
    dve.wait_ge(ln["rstd_done"], g + 1)
    for i in range(GT):
        last = dve.tensor_scalar(out_of(i), tile_of(i), ln["mv"][:, i, 0:1], ln["rstd"][:, i:i + 1],
                                 ALU.subtract, ALU.mult)
    last.then_inc(done, 1)


def gated_ffn_layer(nc, x_sb, const, w_gate, w_up, w_down):
    with ExitStack() as ctx:
        sb, ps, sem = scope(nc, ctx, "ffn")
        wi_gu = sb("wi_gu", [P, 2, KC, HID], I32)
        wi_d = sb("wi_d", [P, MC, C], I32)
        w_gu, w_d = wi_gu[:].bitcast(F32), wi_d[:].bitcast(F32)
        x_norm = sb("x_norm", [P, GT, C])
        xT = sb("xT", [P, 2, KC, GW])
        gated = sb("gated", [P, 2, GW])
        hT = sb("hT", [P, MC, GW])
        z = sb("z", [P, GT, C])
        ps_T = ps("ps_T", [P, KC, GW])
        ps_gate = ps("ps_gate", [P, 2, GW])
        ps_up = ps("ps_up", [P, 2, GW])
        ps_y = ps("ps_y", [P, GT, C])
        ln_in = group_norm(sb, sem, "ln_in", EPS, const)
        ln_out = group_norm(sb, sem, "ln_out", EPS / (SCALE * SCALE), const)
        m = {n: sem(n) for n in ("w_loaded", "w_cast", "normed", "x_turned", "xT_ready", "gate_done",
                                   "up_done", "gate_grown", "h_ready", "y_done", "y_normed", "x_added")}
        eye = const["eye"]

        with nc.Block() as blk:
            @blk.sync
            def _(sp):
                for n, w in enumerate((w_gate, w_up)):
                    sp.dma_start(wi_gu[:, n], w.rearrange("(k p) n -> p k n", p=P)).then_inc(m["w_loaded"], 16)
                sp.dma_start(wi_d[:], w_down.rearrange("(k p) n -> p k n", p=P)).then_inc(m["w_loaded"], 16)

            @blk.gpsimd
            def _(pool):
                norm_power(ln_in, pool, 0)

                def step(g, b, first, last):
                    if not last:
                        norm_power(ln_in, pool, g + 1)
                    norm_power(ln_out, pool, g)
                    pool.wait_ge(m["y_normed"], g + 1)
                    xs = x_sb[:].rearrange("p (g i) c -> p g i c", i=GT)[:, g]
                    pool.tensor_tensor(xs, xs, z[:], ALU.add).then_inc(m["x_added"], 1)

                run_steps(pool, GROUPS, step)

            @blk.vector
            def _(dve):
                def inputs(g):
                    norm_measure(ln_in, dve, lambda i: x_sb[:, g * GT + i, :], g)

                def norm(g):
                    norm_apply(ln_in, dve, lambda i: x_norm[:, i, :], lambda i: x_sb[:, g * GT + i, :], g, m["normed"])

                def step(g, b, first, last):
                    for c in range(MC):
                        if c == 1 and not last:
                            inputs(g + 1)
                        if c == 3 and not last:
                            norm(g + 1)
                        dve.wait_ge(m["gate_grown"], g * MC + c + 1)
                        dve.wait_ge(m["up_done"], g * MC + c + 1)
                        dve.scalar_tensor_tensor(hT[:, c, :], ps_up[:, c % 2, :], SCALE, gated[:, c % 2, :],
                                                 ALU.mult, ALU.mult).then_inc(m["h_ready"], 1)
                    dve.wait_ge(m["y_done"], g + 1)
                    norm_measure(ln_out, dve, lambda i: ps_y[:, i, :], g)
                    if not first:
                        dve.wait_ge(m["x_added"], g)
                    norm_apply(ln_out, dve, lambda i: z[:, i, :], lambda i: ps_y[:, i, :], g, m["y_normed"])

                inputs(0)
                norm(0)
                dve.wait_ge(m["w_loaded"], 48)
                for n in range(2):
                    dve.tensor_copy(w_gu[:, n], wi_gu[:, n]).then_inc(m["w_cast"], 1)
                dve.tensor_copy(w_d, wi_d[:]).then_inc(m["w_cast"], 1)
                run_steps(dve, GROUPS, step)

            @blk.scalar
            def _(act):
                def turned(g, b):
                    act.wait_ge(m["x_turned"], g + 1)
                    for k in range(KC):
                        last = act.copy(xT[:, b, k, :], ps_T[:, k, :])
                    last.then_inc(m["xT_ready"], 1)

                def step(g, b, first, last):
                    for c in range(MC):
                        if c == MC - 1 and not last:
                            turned(g + 1, 1 - b)
                        act.wait_ge(m["gate_done"], g * MC + c + 1)
                        if not (first and c < 2):
                            act.wait_ge(m["h_ready"], g * MC + c - 1)
                        act.activation(gated[:, c % 2, :], ps_gate[:, c % 2, :], ACT.Silu,
                                       scale=SCALE).then_inc(m["gate_grown"], 1)

                turned(0, 0)
                run_steps(act, GROUPS, step)

            @blk.tensor
            def _(pe):
                def turn(g):
                    pe.wait_ge(m["normed"], g + 1)
                    for k in range(KC):
                        for i in range(GT):
                            last = pe.transpose(ps_T[:, k, i * P:(i + 1) * P], x_norm[:, i, k * P:(k + 1) * P], eye)
                    last.then_inc(m["x_turned"], 1)

                def step(g, b, first, last):
                    pe.wait_ge(m["xT_ready"], g + 1)
                    for c in range(MC):
                        if c == MC - 2 and not last:
                            turn(g + 1)
                        if not (first and c < 2):
                            pe.wait_ge(m["h_ready"], g * MC + c - 1)
                        for n, (ps, done) in enumerate(((ps_gate, "gate_done"), (ps_up, "up_done"))):
                            for k in range(KC):
                                mm = pe.matmul(ps[:, c % 2, :], w_gu[:, n, k, c * P:(c + 1) * P], xT[:, b, k, :],
                                               start=(k == 0), stop=(k == KC - 1))
                            mm.then_inc(m[done], 1)
                    pe.wait_ge(m["h_ready"], (g + 1) * MC)
                    if not first:
                        pe.wait_ge(m["y_normed"], g)
                    for i in range(GT):
                        for c in range(MC):
                            mm = pe.matmul(ps_y[:, i, :], hT[:, c, i * P:(i + 1) * P], w_d[:, c, :],
                                           start=(c == 0), stop=(c == MC - 1))
                    mm.then_inc(m["y_done"], 1)

                turn(0)
                pe.wait_ge(m["w_cast"], 3)
                run_steps(pe, GROUPS, step)


HEADS2 = 2 * NH
LEAF = 32
SLOTS_Q = (0, 0, 1, 1, 0, 2)
SLOTS_K = (0, 1, 0, 1, 2, 0)
NSLOT = len(SLOTS_Q)
KROWS = NSLOT * HD


def run_pairs(eng, n, step):
    step(0, 0, 0, True, False)
    with eng.Fori(0, (n - 2) // 2) as i:
        for j in range(2):
            step(2 * i + 1 + j, (1 + j) % 2, i + (1 + j) // 2, False, False)
    step(n - 1, (n - 1) % 2, (n - 1) // 2, False, True)


def rotary_projection(nc, x_sb, x_rest, const, w_qkv, b_qkv, parts, v_sb, qk_own):
    with ExitStack() as ctx:
        sb, ps, sem = scope(nc, ctx, "rot")
        w = sb("w", [P, KC, 3 * C])
        bias = sb("bias", [P, 3 * C])
        x_norm = sb("x_norm", [P, GT, C])
        xT = sb("xT", [P, 2, KC, GW])
        qk = sb("qk", [P, 2, 2 * C])
        rot = sb("rot", [P, 2 * NH, HD // 4])
        rot2 = sb("rot2", [P, 2 * NH, HD // 4])
        prod = sb("prod", [P, C])
        rest = sb("rest", [P, 2, 4, P])
        stage = sb("stage", [P, 2, 3, 4, GW], BF16)
        ps_T = ps("ps_T", [P, KC, GW])
        ps_qk = ps("ps_qk", [P, 2, 2 * C])
        ps_v = ps("ps_v", [P, 2, 512])
        ps_r = ps("ps_r", [P, 2, 4, P])
        ln_in = group_norm(sb, sem, "ln_in", EPS, const)
        m = {n: sem(n) for n in ("w_loaded", "x_stored", "bias_scaled", "normed", "x_turned", "xT_ready",
                                   "projected", "qk_biased", "v_biased", "turning", "rotated", "multiplied",
                                   "own_done", "qk_turned", "high_done", "rest_done", "mid_done", "low_done")}
        parts_stored = [sem(f"parts_stored{b}") for b in range(2)]
        eye, cos, sin = const["eye"], const["cos"], const["sin"]
        R = HD // 4

        with nc.Block() as blk:
            @blk.sync
            def _(sp):
                sp.dma_start(w[:], w_qkv.rearrange("(k p) n -> p k n", p=P)).then_inc(m["w_loaded"], 16)
                sp.dma_start(bias[:], b_qkv).then_inc(m["w_loaded"], 16)
                sp.dma_start(x_rest, x_sb[:]).then_inc(m["x_stored"], 16)

                def step(g, b, pair, first, last):
                    sp.wait_ge(m["low_done"], (g + 1) * GT)
                    sp.dma_start(parts.rearrange("a p (g t) -> g p a t", t=GW)[g],
                                 stage[:, b].rearrange("p s o t -> p (s o) t")).then_inc(parts_stored[b], 16)

                run_pairs(sp, GROUPS, step)
                for b in range(2):
                    sp.wait_ge(parts_stored[b], 16 * (GROUPS // 2 + 1))
                sp.wait_ge(m["x_stored"], 16)

            @blk.gpsimd
            def _(pool):
                norm_power(ln_in, pool, 0)

                def rotate(n, b, i):
                    c, j = i % 2, b * GT + i
                    r = qk[:, c].rearrange("p (h d) -> p h d", d=HD)
                    cs, sn = cos[:, j * R:(j + 1) * R], sin[:, j * R:(j + 1) * R]
                    half = R // 2

                    def over(v):
                        return v.unsqueeze(1).broadcast_to([P, 2 * NH, v.shape[1]])

                    pool.wait_ge(m["qk_biased"], n + 1)
                    pool.tensor_tensor(rot[:], r[:, :, 0:R], over(cs), ALU.mult).then_inc(m["turning"], 1)
                    pool.tensor_tensor(rot2[:, :, 0:half], r[:, :, half:R], over(sn[:, 0:half]), ALU.mult
                                       ).then_inc(m["turning"], 1)
                    pool.tensor_tensor(rot2[:, :, half:R], r[:, :, 0:half], over(sn[:, half:R]), ALU.mult
                                       ).then_inc(m["turning"], 1)
                    pool.wait_ge(m["turning"], 3 * n + 3)
                    pool.tensor_tensor(r[:, :, 0:R], rot[:], rot2[:], ALU.add).then_inc(m["rotated"], 1)
                    pool.wait_ge(m["rotated"], n + 1)
                    if not (isinstance(n, int) and n == 0):
                        pool.wait_ge(m["own_done"], n)
                    pool.tensor_tensor(prod[:], qk[:, c, 0:C], qk[:, c, C:2 * C], ALU.mult).then_inc(m["multiplied"], 1)

                def step(g, b, pair, first, last):
                    for i in range(GT):
                        n = g * GT + i
                        rotate(n, b, i)
                        if i == 2 and not last:
                            norm_power(ln_in, pool, g + 1)

                run_pairs(pool, GROUPS, step)

            @blk.vector
            def _(dve):
                def inputs(g):
                    norm_measure(ln_in, dve, lambda i: x_sb[:, g * GT + i, :], g)

                def norm(g):
                    norm_apply(ln_in, dve, lambda i: x_norm[:, i, :], lambda i: x_sb[:, g * GT + i, :], g, m["normed"])

                def biases(n, b, pair, i):
                    c = i % 2
                    dve.wait_ge(m["projected"], n + 1)
                    if not (isinstance(n, int) and n < 2):
                        dve.wait_ge(m["qk_turned"], n - 1)
                        dve.wait_ge(m["multiplied"], n - 1)
                    dve.scalar_tensor_tensor(qk[:, c, 0:C], ps_qk[:, c, 0:C], HD ** -0.5, bias[:, 0:C],
                                             ALU.mult, ALU.add)
                    dve.tensor_tensor(qk[:, c, C:2 * C], ps_qk[:, c, C:2 * C], bias[:, C:2 * C],
                                      ALU.add).then_inc(m["qk_biased"], 1)
                    dve.tensor_tensor(v_sb[:, b * GT + i, pair, :], ps_v[:, c, 0:C], bias[:, 2 * C:3 * C],
                                      ALU.add).then_inc(m["v_biased"], 1)

                def parts_of(n, b, pair, i):
                    dve.wait_ge(m["multiplied"], n + 1)
                    dve.tensor_reduce(qk_own[:, b * GT + i, pair, :], prod[:].rearrange("p (h d) -> p h d", d=HD),
                                      AX, ALU.add).then_inc(m["own_done"], 1)
                    dve.wait_ge(m["high_done"], n + 1)
                    if not (isinstance(n, int) and n < 2):
                        dve.wait_ge(m["low_done"], n - 1)
                    dve.tensor_tensor(rest[:, i % 2], ps_r[:, i % 2], stage[:, b, 0, :, i * P:(i + 1) * P],
                                      ALU.subtract).then_inc(m["rest_done"], 1)

                def low(n, b, i):
                    dve.wait_ge(m["mid_done"], n + 1)
                    dve.tensor_tensor(stage[:, b, 2, :, i * P:(i + 1) * P], rest[:, i % 2],
                                      stage[:, b, 1, :, i * P:(i + 1) * P], ALU.subtract).then_inc(m["low_done"], 1)

                def step(g, b, pair, first, last):
                    for i in range(GT):
                        n = g * GT + i
                        biases(n, b, pair, i)
                        if i:
                            parts_of(n - 1, b, pair, i - 1)
                        if i > 1:
                            low(n - 2, b, i - 2)
                        if i == 1 and not last:
                            inputs(g + 1)
                        if i == 2 and not last:
                            norm(g + 1)
                    low(g * GT + GT - 2, b, GT - 2)
                    parts_of(g * GT + GT - 1, b, pair, GT - 1)
                    low(g * GT + GT - 1, b, GT - 1)

                dve.wait_ge(m["w_loaded"], 32)
                dve.tensor_scalar(bias[:, 0:C], bias[:, 0:C], HD ** -0.5, None, ALU.mult
                                  ).then_inc(m["bias_scaled"], 1)
                dve.wait_ge(m["bias_scaled"], 1)
                inputs(0)
                norm(0)
                run_pairs(dve, GROUPS, step)

            @blk.scalar
            def _(act):
                def turned(g, b):
                    act.wait_ge(m["x_turned"], g + 1)
                    for k in range(KC):
                        last = act.copy(xT[:, b, k, :], ps_T[:, k, :])
                    last.then_inc(m["xT_ready"], 1)

                def high(n, b, i):
                    act.wait_ge(m["qk_turned"], n + 1)
                    act.copy(stage[:, b, 0, :, i * P:(i + 1) * P], ps_r[:, i % 2]).then_inc(m["high_done"], 1)

                def mid(n, b, i):
                    act.wait_ge(m["rest_done"], n + 1)
                    act.copy(stage[:, b, 1, :, i * P:(i + 1) * P], rest[:, i % 2]).then_inc(m["mid_done"], 1)

                def step(g, b, pair, first, last):
                    act.wait_ge(parts_stored[b], 16 * (pair + 1))
                    for i in range(GT):
                        n = g * GT + i
                        high(n, b, i)
                        mid(n, b, i)
                        if i == GT - 2 and not last:
                            turned(g + 1, 1 - b)

                turned(0, 0)
                for b in range(2):
                    act.sem_inc(parts_stored[b], 16)
                run_pairs(act, GROUPS, step)

            @blk.tensor
            def _(pe):
                def turn(g):
                    pe.wait_ge(m["normed"], g + 1)
                    for k in range(KC):
                        for i in range(GT):
                            last = pe.transpose(ps_T[:, k, i * P:(i + 1) * P], x_norm[:, i, k * P:(k + 1) * P], eye)
                    last.then_inc(m["x_turned"], 1)

                def project(n, b, i):
                    c = i % 2
                    if not (isinstance(n, int) and n < 2):
                        pe.wait_ge(m["v_biased"], n - 1)
                    for ps, a, e in ((ps_qk[:, c, :], 0, 2 * C), (ps_v[:, c, 0:C], 2 * C, 3 * C)):
                        for k in range(KC):
                            mm = pe.matmul(ps, xT[:, b, k, i * P:(i + 1) * P], w[:, k, a:e],
                                           start=(k == 0), stop=(k == KC - 1))
                    mm.then_inc(m["projected"], 1)

                def turn_qk(n, i):
                    c = i % 2
                    pe.wait_ge(m["rotated"], n + 1)
                    if not (isinstance(n, int) and n < 2):
                        pe.wait_ge(m["rest_done"], n - 1)
                    for o in range(4):
                        mm = pe.transpose(ps_r[:, c, o, :], qk[:, c, o * P:(o + 1) * P], eye)
                    mm.then_inc(m["qk_turned"], 1)

                def step(g, b, pair, first, last):
                    pe.wait_ge(m["xT_ready"], g + 1)
                    for i in range(GT):
                        project(g * GT + i, b, i)
                        if i:
                            turn_qk(g * GT + i - 1, i - 1)
                        if i == 2 and not last:
                            turn(g + 1)
                    turn_qk(g * GT + GT - 1, GT - 1)

                pe.wait_ge(m["w_loaded"], 32)
                turn(0)
                run_pairs(pe, GROUPS, step)


def softmax_and_solve(nc, x_sb, const, parts, a_sb, qk_own):
    NB = TPB
    with ExitStack() as ctx:
        sb, ps, sem = scope(nc, ctx, "att")
        k_all = sb("k_all", [KROWS + 3, HEADS2, SEQ], BF16)
        q_blk = sb("q_blk", [KROWS + 3, 4, HEADS2, P], BF16)
        eye_b = sb("eye_b", [P, P], BF16)
        bias_b = sb("bias_b", [P, P], BF16)
        probs_T = sb("probs_T", [P, 2, SEQ])
        own_T = [x_sb[:, b * TILES // 2:(b + 1) * TILES // 2, :].rearrange("p t (z c) -> p (t z) c", c=P)
                 for b in range(2)]
        neg_max = sb("neg_max", [P, HEADS2])
        total = sb("total", [P, HEADS2])
        ln_total = sb("ln_total", [P, HEADS2])
        shift = sb("shift", [P, HEADS2])
        shift_rest = sb("shift_rest", [HEADS2, P])
        shift_parts = sb("shift_parts", [HEADS2, 3, P], BF16)
        own_log = sb("own_log", [P, HEADS2])
        own_prob = sb("own_prob", [P, HEADS2])
        leaf_T = sb("leaf_T", [P, HEADS2, LEAF])
        leaf = sb("leaf", [P, LEAF, LEAF])
        inverse = sb("inverse", [P, LEAF, LEAF])
        inverse_T = sb("inverse_T", [P, LEAF, HEADS2])
        outer = sb("outer", [P, 256])
        rhs_v = sb("rhs_v", [P, 2, HEADS2, HD])
        u_T = sb("u_T", [P, 2, 4, P])
        rhs = sb("rhs", [P, HEADS2, HD])
        solved = sb("solved", [P, HEADS2, HD])
        ps_s = ps("ps_s", [P, 2, SEQ])
        ps_u = ps("ps_u", [P, 2, 4, P])
        ps_g = ps("ps_g", [P, HEADS2, HD])
        ps_x = ps("ps_x", [HEADS2, P])
        names = ("const_ready", "ones_set", "scored", "maxed", "job_done", "earlier_done", "logged",
                 "shifted", "shift_turned", "split_step", "parts_ready", "shift_in", "own_logged", "own_grown", "u_taken", "u_turned",
                 "v_weighted", "leaves_out", "leaves_in", "eye_step", "leaf_step", "inverse_taken",
                 "rhs_ready", "partial_done", "rows_done", "rows_copied", "a_written")
        m = {n: sem(n) for n in names}
        passed = const["passed"]
        k_loaded = [sem(f"k_loaded{b}") for b in range(2)]
        q_loaded = [sem(f"q_loaded{b}") for b in range(4)]
        eye = const["eye"]
        KQ = KROWS + 3
        PER_JOB = [0, 8, 4, 2, 2, 1, 1, 1]
        OWN_JOBS = HEADS2 * P // SEQ
        JOBS = [HEADS2 // n if n else 0 for n in PER_JOB]
        M_AT, O_AT, B_AT, E_AT = {}, {}, {}, {}
        at = e_at = 0
        M_AT[0], O_AT[0], M_AT[1] = 0, HEADS2, HEADS2 + OWN_JOBS
        at = 2 * HEADS2 + OWN_JOBS
        for i in range(NB):
            B_AT[i], E_AT[i] = at, e_at
            at, e_at = at + JOBS[i], e_at + JOBS[i]
            if i + 1 < NB:
                O_AT[i + 1] = at
                at += OWN_JOBS
            if i + 2 < NB:
                M_AT[i + 2] = at
                at += HEADS2
        JH, EH = at, e_at

        def beside(half, i):
            if i + 2 < NB:
                return half, i + 2
            return (1, 0) if (half, i) == (0, NB - 1) else None

        STEPS = 2 * (LEAF - 1)

        def u_of(head):
            x, g, c = head // NH, head % NH // 4, head % 4
            return ps_u[c * LEAF:c * LEAF + HD, x, g, :]

        def room(n, W):
            return ps_s[:, n % 3, 0:W] if n % 3 < 2 else ps_u[:].rearrange("p x g q -> p (x g q)")[:, 0:W]

        def exps(n, W):
            return probs_T[:, n % 3, 0:W] if n % 3 < 2 else u_T[:].rearrange("p x g q -> p (x g q)")[:, 0:W]

        def rows_of(q):
            return slice(q * LEAF, (q + 1) * LEAF)

        with nc.Block() as blk:
            @blk.sync
            def _(sp):
                src = parts.rearrange("(s w o) p t -> s w (o p) t", s=3, w=2).rearrange(
                    "s w (h d) (b t) -> s w b d h t", d=HD, b=BATCH)

                def load_q(half, i):
                    for n in range(NSLOT):
                        for b2 in range(2):
                            sp.dma_start(q_blk[n * HD:(n + 1) * HD, i % 4, b2 * NH:(b2 + 1) * NH, :],
                                         src[SLOTS_Q[n], 0, half * 2 + b2][:, :, i * P:(i + 1) * P]
                                         ).then_inc(q_loaded[i % 4], 16)

                def shift_rows(half, i):
                    sp.wait_ge(m["parts_ready"], half * NB + i + 1)
                    for s in range(3):
                        sp.dma_start(q_blk[KROWS + s:KROWS + s + 1, i % 4],
                                     shift_parts[:, s]).then_inc(m["shift_in"], 16)

                for half in range(2):
                    if half:
                        sp.wait_ge(m["rows_done"], 4 * 5)
                    load_q(half, 0)
                    for b2 in range(2):
                        sp.wait_ge(m["earlier_done"], half * EH - (1 - b2) * half * JOBS[NB - 1] // 2 + 2)
                        for n in range(NSLOT):
                            sp.dma_start(k_all[n * HD:(n + 1) * HD, b2 * NH:(b2 + 1) * NH, :],
                                         src[SLOTS_K[n], 1, half * 2 + b2]).then_inc(k_loaded[b2], 16)
                    load_q(half, 1)
                    load_q(half, 2)
                    shift_rows(half, 0)
                    shift_rows(half, 1)
                    for i in range(NB):
                        if i + 3 < NB:
                            if i:
                                sp.wait_ge(m["rows_done"], half * 4 * NB + 4 * i)
                            load_q(half, i + 3)
                        if i + 2 < NB:
                            shift_rows(half, i + 2)

            @blk.gpsimd
            def _(pool):
                pool.memset(k_all[KROWS:KQ].rearrange("p h t -> p (h t)"), 1.0).then_inc(m["ones_set"], 1)
                pool.wait_ge(m["ones_set"], 1)
                pool.sem_inc(m["inverse_taken"], 1)
                for half in range(2):
                    for i in range(NB):
                        p = half * NB + i
                        hold(pool, m["inverse_taken"], p + 1, passed)
                        flat = inverse[:].rearrange("p a b -> p (a b)")
                        pool.memset(flat, 0.0).then_inc(m["eye_step"], 1)
                        hold(pool, m["eye_step"], 2 * p + 1, passed)
                        pool.memset(flat[:, ::LEAF + 1], 1.0).then_inc(m["eye_step"], 1)
                        pool.wait_ge(m["eye_step"], 2 * p + 2)
                        pool.wait_ge(m["leaves_in"], p + 2)
                        for k in range(LEAF - 1):
                            below, w = LEAF - 1 - k, k + 1
                            t = outer[:, 0:below * w].rearrange("p (i j) -> p i j", j=w)
                            pool.tensor_tensor(t, leaf[:, k + 1:LEAF, k].unsqueeze(2).broadcast_to([P, below, w]),
                                               inverse[:, k, 0:w].unsqueeze(1).broadcast_to([P, below, w]),
                                               ALU.mult).then_inc(m["leaf_step"], 1)
                            pool.wait_ge(m["leaf_step"], p * STEPS + 2 * k + 1)
                            pool.tensor_tensor(inverse[:, k + 1:LEAF, 0:w], inverse[:, k + 1:LEAF, 0:w], t,
                                               ALU.add).then_inc(m["leaf_step"], 1)
                            if k < LEAF - 2:
                                pool.wait_ge(m["leaf_step"], p * STEPS + 2 * k + 2)

            @blk.vector
            def _(dve):
                def row_max(half, i, n):
                    dve.wait_ge(m["scored"], half * JH + M_AT[i] + n + 1)
                    dve.tensor_reduce(neg_max[:, bass.ds(n, 1)], room(n, (i + 1) * P), AX, ALU.max,
                                      negate=True).then_inc(m["maxed"], 1)

                def make_shift(half, i):
                    p = half * NB + i
                    dve.wait_ge(m["logged"], p + 1)
                    dve.tensor_tensor(shift[:], neg_max[:], ln_total[:], ALU.subtract).then_inc(m["shifted"], 1)
                    dve.wait_ge(m["shifted"], p + 1)
                    own = qk_own[:, i].rearrange("p (x b) h -> p x (b h)", x=2)[:, half]
                    dve.tensor_tensor(own_log[:], own, shift[:], ALU.add).then_inc(m["own_logged"], 1)
                    dve.wait_ge(m["shift_turned"], p + 1)
                    dve.wait_ge(m["shift_in"], 48 * p + 48)
                    dve.tensor_copy(shift_parts[:, 0], ps_x[:]).then_inc(m["split_step"], 1)
                    dve.wait_ge(m["split_step"], 3 * p + 1)
                    dve.tensor_tensor(shift_rest[:], ps_x[:], shift_parts[:, 0], ALU.subtract
                                      ).then_inc(m["split_step"], 1)
                    dve.wait_ge(m["split_step"], 3 * p + 2)
                    dve.tensor_copy(shift_parts[:, 1], shift_rest[:]).then_inc(m["split_step"], 1)
                    dve.wait_ge(m["split_step"], 3 * p + 3)
                    dve.tensor_tensor(shift_parts[:, 2], shift_rest[:], shift_parts[:, 1], ALU.subtract
                                      ).then_inc(m["parts_ready"], 1)
                    dve.wait_ge(m["own_grown"], p + 1)
                    v = a_half(half, i).rearrange("p (h d) -> p h d", d=HD)
                    dve.tensor_tensor(rhs_v[:, i % 2], v, own_prob[:].unsqueeze(2).broadcast_to([P, HEADS2, HD]),
                                      ALU.mult).then_inc(m["v_weighted"], 1)

                def a_half(half, i):
                    return a_sb[:, i].rearrange("p (x b) c -> p x (b c)", x=2)[:, half]

                def take_leaves(half, i):
                    p = half * NB + i
                    dve.wait_ge(m["leaves_out"], p + 1)
                    dve.transpose(leaf[:].rearrange("p i j -> p (i j)"), leaf_T[:].rearrange("p h i -> p i h")
                                  ).then_inc(m["leaves_in"], 1)

                def take_inverse(half, i):
                    p = half * NB + i
                    dve.wait_ge(m["leaf_step"], (p + 1) * STEPS)
                    dve.transpose(inverse_T[:].rearrange("p i h -> p (i h)"), inverse[:].rearrange("p i j -> p (i j)")
                                  ).then_inc(m["inverse_taken"], 1)

                def right_side(half, i, q):
                    p, r = half * NB + i, rows_of(q)
                    if q:
                        dve.wait_ge(m["partial_done"], p * 3 + q)
                        last = dve.tensor_tensor(rhs[r], ps_g[r], rhs[r], ALU.add)
                    else:
                        dve.wait_ge(m["v_weighted"], p + 1)
                        if i:
                            dve.wait_ge(m["u_turned"], (NB - 1) * half + i)
                            for x in range(2):
                                h = slice(x * NH, (x + 1) * NH)
                                u = ps_u[:, x].rearrange("p g (c w) -> p (g c) w", w=LEAF)[:, :, 0:HD]
                                last = dve.tensor_tensor(rhs[:, h], u, rhs_v[:, i % 2, h], ALU.add)
                        else:
                            last = dve.tensor_copy(rhs[:], rhs_v[:, i % 2])
                    last.then_inc(m["rhs_ready"], 1)

                def keep_rows(half, i, q):
                    p, r = half * NB + i, rows_of(q)
                    dve.wait_ge(m["rows_done"], p * 4 + q + 1)
                    dve.tensor_copy(solved[r], ps_g[r]).then_inc(m["rows_copied"], 1)

                dve.tensor_copy(eye_b[:], eye).then_inc(m["const_ready"], 1)
                dve.tensor_copy(bias_b[:], const["causal_bias"]).then_inc(m["const_ready"], 1)
                dve.memset(ps_u[:].rearrange("p x g q -> p (x g q)"), 0.0).then_inc(m["const_ready"], 1)
                dve.sem_inc(m["shift_in"], 48)
                dve.sem_inc(m["leaves_in"], 1)
                for half in range(2):
                    if half == 0:
                        for n in range(HEADS2):
                            row_max(half, 0, n)
                    make_shift(half, 0)
                    take_leaves(half, 0)
                    for n in range(HEADS2):
                        row_max(half, 1, n)
                    make_shift(half, 1)
                    for i in range(NB):
                        take_inverse(half, i)
                        for q in range(4):
                            right_side(half, i, q)
                            if q == 0 and i + 1 < NB:
                                take_leaves(half, i + 1)
                            for n in range(8):
                                if n == 3:
                                    keep_rows(half, i, q)
                                if beside(half, i):
                                    row_max(*beside(half, i), 8 * q + n)
                        if i + 2 < NB:
                            make_shift(half, i + 2)

            @blk.scalar
            def _(act):
                def sum_exp(half, i, n):
                    act.wait_ge(m["maxed"], (half * NB + i) * HEADS2 + n + 1)
                    c = bass.ds(n, 1)
                    act.activation(exps(n, (i + 1) * P), room(n, (i + 1) * P), ACT.Exp,
                                   bias=neg_max[:, c], accum_out=total[:, c]).then_inc(m["job_done"], 1)

                def logarithm(half, i):
                    p = half * NB + i
                    act.wait_ge(m["job_done"], half * JH + M_AT[i] + HEADS2 + 2)
                    act.activation(ln_total[:], total[:], ACT.Ln).then_inc(m["logged"], 1)
                    act.wait_ge(m["own_logged"], p + 1)
                    act.activation(own_prob[:], own_log[:], ACT.Exp).then_inc(m["own_grown"], 1)

                def own(half, i):
                    for g in range(OWN_JOBS):
                        act.wait_ge(m["scored"], half * JH + O_AT[i] + g + 1)
                        h = slice(g * HEADS2 // OWN_JOBS, (g + 1) * HEADS2 // OWN_JOBS)
                        act.activation(own_T[i % 2][:, h, :].rearrange("p h q -> p (h q)"), ps_s[:, g % 2],
                                       ACT.Exp).then_inc(m["job_done"], 1)
                    act.wait_ge(m["job_done"], half * JH + O_AT[i] + OWN_JOBS + 2)
                    act.wait_ge(m["leaves_in"], half * NB + i + 1)
                    for q in range(4):
                        r = rows_of(q)
                        last = act.copy(leaf_T[r], own_T[i % 2][r, :, q * LEAF:(q + 1) * LEAF])
                    last.then_inc(m["leaves_out"], 1)

                def earlier(half, i):
                    w, J = PER_JOB[i] * i * P, JOBS[i]

                    def take_products(x):
                        act.wait_ge(m["earlier_done"], half * EH + E_AT[i] + (x + 1) * J // 2 + 2)
                        act.copy(u_T[:, x], ps_u[:, x]).then_inc(m["u_taken"], 1)

                    for n in range(J):
                        k = n % 2
                        act.wait_ge(m["scored"], half * JH + B_AT[i] + n + 1)
                        act.wait_ge(m["earlier_done"], half * EH + E_AT[i] + n + 1)
                        act.activation(probs_T[:, k, 0:w], ps_s[:, k, 0:w], ACT.Exp).then_inc(m["job_done"], 1)
                        if n == J // 2 + 1:
                            take_products(0)
                    take_products(1)

                act.sem_inc(m["job_done"], 2)
                for half in range(2):
                    if half == 0:
                        for n in range(HEADS2):
                            sum_exp(half, 0, n)
                    logarithm(half, 0)
                    own(half, 0)
                    for n in range(HEADS2):
                        sum_exp(half, 1, n)
                    logarithm(half, 1)
                    for i in range(NB):
                        if i:
                            earlier(half, i)
                        if i + 1 < NB:
                            own(half, i + 1)
                        if beside(half, i):
                            for n in range(HEADS2):
                                sum_exp(*beside(half, i), n)
                        act.wait_ge(m["rows_copied"], (half * NB + i) * 4 + 4)
                        a = a_sb[:, i].rearrange("p (x b) c -> p x (b c)", x=2)[:, half]
                        act.copy(a, solved[:].rearrange("p h d -> p (h d)")).then_inc(m["a_written"], 1)
                        if i + 2 < NB:
                            logarithm(half, i + 2)

            @blk.tensor
            def _(pe):
                def free(half, job):
                    pe.wait_ge(m["job_done"], half * JH + job + 1)

                def measure(half, i, n):
                    W = (i + 1) * P
                    if n < 3:
                        free(half, M_AT[i] + n)
                    else:
                        pe.wait_ge(m["job_done"], half * JH + M_AT[i] + n)
                    out = room(n, W)
                    for c in range(0, W, 512):
                        w = min(512, W - c)
                        own = c + w == W
                        mm = pe.matmul(out[:, c:c + w], q_blk[0:KROWS, i % 4, n, :],
                                       k_all[0:KROWS, n, c:c + w], start=True, stop=not own)
                        if own:
                            mm = pe.matmul(out[:, W - P:W], eye_b[:], bias_b[:], start=False, stop=True)
                    mm.then_inc(m["scored"], 1)

                def turn_shift(half, i):
                    pe.wait_ge(m["shifted"], half * NB + i + 1)
                    pe.transpose(ps_x[:], shift[:], eye).then_inc(m["shift_turned"], 1)

                def own(half, i):
                    n = HEADS2 // OWN_JOBS
                    pe.wait_ge(m["ones_set"], 1)
                    pe.wait_ge(m["shift_in"], 48 * (half * NB + i) + 96)
                    for g in range(OWN_JOBS):
                        free(half, O_AT[i] + g)
                        for h in range(n):
                            out = ps_s[:, g % 2, h * P:(h + 1) * P]
                            pe.matmul(out, k_all[:, g * n + h, i * P:(i + 1) * P], q_blk[:, i % 4, g * n + h, :],
                                      start=True, stop=False)
                            mm = pe.matmul(out, bias_b[:], eye_b[:], start=False, stop=True)
                        mm.then_inc(m["scored"], 1)

                def earlier(half, i):
                    per = PER_JOB[i]

                    def scores(n, k):
                        free(half, B_AT[i] + n)
                        for h in range(per):
                            for j in range(i):
                                at = (h * i + j) * P
                                mm = pe.matmul(ps_s[:, k, at:at + P], k_all[:, n * per + h, j * P:(j + 1) * P],
                                               q_blk[:, i % 4, n * per + h, :], start=True, stop=True)
                        mm.then_inc(m["scored"], 1)

                    def products(n, k):
                        for h in range(per):
                            for j in range(i):
                                at = (h * i + j) * P
                                head = n * per + h
                                a = a_sb[:, j].rearrange("p b (h d) -> p (b h) d", d=HD)[:, half * HEADS2 + head, :]
                                mm = pe.matmul(u_of(head), a, probs_T[:, k, at:at + P],
                                               start=(j == 0), stop=(j == i - 1))
                        mm.then_inc(m["earlier_done"], 1)

                    pe.wait_ge(m["a_written"], half * NB + i)
                    scores(0, 0)
                    scores(1, 1)
                    J = JOBS[i]
                    for n in range(J - 2):
                        scores(n + 2, n % 2)
                        products(n, n % 2)
                        if n == 1 and i + 1 < NB:
                            turn_shift(half, i + 1)
                    for n in range(J - 2, J):
                        pe.wait_ge(m["job_done"], half * JH + B_AT[i] + n + 3)
                        products(n, n % 2)
                    for x in range(2):
                        pe.wait_ge(m["u_taken"], ((NB - 1) * half + i - 1) * 2 + x + 1)
                        for g in range(4):
                            mm = pe.transpose(ps_u[:, x, g, :], u_T[:, x, g, :], eye)
                    mm.then_inc(m["u_turned"], 1)

                def solve_and_measure(half, i):
                    p = half * NB + i

                    def more(n):
                        if beside(half, i):
                            if beside(half, i) == (1, 0) and n % NH == 0:
                                pe.wait_ge(k_loaded[n // NH], 2 * 16 * NSLOT)
                            measure(*beside(half, i), n)

                    for q in range(4):
                        r = rows_of(q)
                        if q == 0:
                            hold(pe, m["inverse_taken"], p + 2, passed)
                        hold(pe, m["rhs_ready"], p * 4 + q + 1, passed)
                        for h in range(HEADS2):
                            mm = pe.matmul(ps_g[r, h, :], inverse_T[r, :, h], rhs[r, h, :], start=True, stop=True)
                            if h % 8 == 7:
                                if h == HEADS2 - 1:
                                    mm.then_inc(m["rows_done"], 1)
                                more(8 * q + h // 8)
                        if q < 3:
                            r2 = rows_of(q + 1)
                            hold(pe, m["rows_copied"], p * 4 + q + 1, passed)
                            for h in range(HEADS2):
                                mm = pe.matmul(ps_g[r2, h, :], own_T[i % 2][0:(q + 1) * LEAF, h, r2],
                                               solved[0:(q + 1) * LEAF, h, :], start=True, stop=True)
                                if h % 8 == 7:
                                    if h == HEADS2 - 1:
                                        mm.then_inc(m["partial_done"], 1)
                                    more(8 * q + 4 + h // 8)
                        else:
                            for n in range(4):
                                more(28 + n)

                pe.sem_inc(m["earlier_done"], 2)
                pe.wait_ge(m["const_ready"], 3)
                for half in range(2):
                    if half == 0:
                        pe.wait_ge(q_loaded[0], 16 * NSLOT * 2)
                        for n in range(HEADS2):
                            if n % NH == 0:
                                pe.wait_ge(k_loaded[n // NH], 16 * NSLOT)
                            measure(half, 0, n)
                    for b in (1, 2):
                        pe.wait_ge(q_loaded[b], (2 * half + 1) * 16 * NSLOT * 2)
                    turn_shift(half, 0)
                    own(half, 0)
                    for n in range(HEADS2):
                        measure(half, 1, n)
                    turn_shift(half, 1)
                    for i in range(NB):
                        if i:
                            earlier(half, i)
                        if i + 1 < NB:
                            own(half, i + 1)
                        if (half, i) == (0, NB - 1):
                            pe.wait_ge(q_loaded[0], 3 * 16 * NSLOT * 2)
                        if 1 <= i < NB - 2:
                            n_before = (i + 2) // 4
                            pe.wait_ge(q_loaded[(i + 2) % 4], (half * 2 + n_before + 1) * 16 * NSLOT * 2)
                        solve_and_measure(half, i)


def output_projection(nc, x_sb, x_rest, const, w_out, b_out, a_sb):
    with ExitStack() as ctx:
        sb, ps, sem = scope(nc, ctx, "prj")
        w = sb("w", [P, KC, C])
        bias = sb("bias", [P, C])
        a_grp = sb("a_grp", [P, 2, GT, C])
        aT = sb("aT", [P, 2, KC, GW])
        y = sb("y", [P, GT, C])
        z = sb("z", [P, GT, C])
        ps_T = ps("ps_T", [P, KC, GW])
        ps_y = ps("ps_y", [P, 2, GT, C])
        ln_out = group_norm(sb, sem, "ln_out", EPS, const)
        x_loaded = [sem(f"x_loaded{b}") for b in range(2)]
        m = {n: sem(n) for n in ("w_loaded", "a_ready", "a_turned", "aT_ready", "y_done", "y_biased",
                                   "y_normed", "x_added")}
        eye = const["eye"]

        with nc.Block() as blk:
            @blk.sync
            def _(sp):
                sp.dma_start(w[:], w_out.rearrange("(k p) n -> p k n", p=P)).then_inc(m["w_loaded"], 16)
                sp.dma_start(bias[:], b_out).then_inc(m["w_loaded"], 16)
                for g in range(GROUPS):
                    if g > 1:
                        sp.wait_ge(x_loaded[g % 2], 16 * (g // 2))
                    tiles = slice(g * GT, (g + 1) * GT)
                    sp.dma_start(x_sb[:, tiles, :], x_rest[:, tiles, :]).then_inc(x_loaded[g % 2], 16)

            @blk.gpsimd
            def _(pool):
                def step(g, b, pair, first, last):
                    norm_power(ln_out, pool, g)
                    pool.wait_ge(m["y_normed"], g + 1)
                    pool.wait_ge(x_loaded[b], 16 * (pair + 1))
                    xs = x_sb[:].rearrange("p (g i) c -> p g i c", i=GT)[:, g]
                    pool.tensor_tensor(xs, xs, z[:], ALU.add).then_inc(m["x_added"], 1)

                run_pairs(pool, GROUPS, step)

            @blk.vector
            def _(dve):
                def step(g, b, pair, first, last):
                    if not first:
                        dve.wait_ge(m["y_normed"], g)
                    dve.wait_ge(m["y_done"], g + 1)
                    dve.tensor_tensor(y[:], ps_y[:, b], bias[:].unsqueeze(1).broadcast_to([P, GT, C]),
                                      ALU.add).then_inc(m["y_biased"], 1)
                    dve.wait_ge(m["y_biased"], g + 1)
                    norm_measure(ln_out, dve, lambda i: y[:, i, :], g)
                    if not first:
                        dve.wait_ge(m["x_added"], g)
                    norm_apply(ln_out, dve, lambda i: z[:, i, :], lambda i: y[:, i, :], g, m["y_normed"])

                dve.wait_ge(m["w_loaded"], 32)
                run_pairs(dve, GROUPS, step)

            @blk.scalar
            def _(act):
                def gather(g, b, pair):
                    if not (isinstance(g, int) and g < 2):
                        act.wait_ge(m["a_turned"], g - 1)
                    act.copy(a_grp[:, b], a_sb[:, b * GT:(b + 1) * GT, pair, :]).then_inc(m["a_ready"], 1)

                def step(g, b, pair, first, last):
                    if not last:
                        gather(g + 1, 1 - b, pair + b)
                    act.wait_ge(m["a_turned"], g + 1)
                    for k in range(KC):
                        last_ = act.copy(aT[:, b, k, :], ps_T[:, k, :])
                    last_.then_inc(m["aT_ready"], 1)

                gather(0, 0, 0)
                run_pairs(act, GROUPS, step)

            @blk.tensor
            def _(pe):
                def turn(g, b):
                    pe.wait_ge(m["a_ready"], g + 1)
                    for k in range(KC):
                        for i in range(GT):
                            mm = pe.transpose(ps_T[:, k, i * P:(i + 1) * P], a_grp[:, b, i, k * P:(k + 1) * P], eye)
                    mm.then_inc(m["a_turned"], 1)

                def step(g, b, pair, first, last):
                    pe.wait_ge(m["aT_ready"], g + 1)
                    if not last:
                        turn(g + 1, 1 - b)
                    if not (isinstance(g, int) and g < 2):
                        pe.wait_ge(m["y_biased"], g - 1)
                    for i in range(GT):
                        for k in range(KC):
                            mm = pe.matmul(ps_y[:, b, i, :], aT[:, b, k, i * P:(i + 1) * P], w[:, k, :],
                                           start=(k == 0), stop=(k == KC - 1))
                    mm.then_inc(m["y_done"], 1)

                turn(0, 0)
                pe.wait_ge(m["w_loaded"], 32)
                run_pairs(pe, GROUPS, step)


NE = 8
NC_R = NE + 1


def moe_layer(nc, x_sb, const, router, w1, w2, s_up, s_down):
    with ExitStack() as ctx:
        sb, ps, sem = scope(nc, ctx, "moe")
        w_r = sb("w_r", [P, KC, NC_R])
        w_1 = sb("w_1", [P, NE, KC, C])
        w_2 = sb("w_2", [P, NE + 1, KC, C])
        w_s = sb("w_s", [P, KC, 2 * C])
        x_norm = sb("x_norm", [P, GT, C])
        xT = sb("xT", [P, 2, KC, GW])
        gated = sb("gated", [P, KC, GW])
        hT = sb("hT", [P, 2, KC, GW])
        logits = sb("logits", [P, GT, NC_R])
        top = sb("top", [P, GT])
        grown = sb("grown", [P, GT, NC_R])
        total = sb("total", [P, GT])
        probs = sb("probs", [P, GT, NE])
        above = sb("above", [P, GT, NE, NE])
        level = sb("level", [P, GT, NE, NE])
        rank = sb("rank", [P, GT, NE])
        comb = sb("comb", [P, 2, GT, NC_R])
        acc = sb("acc", [P, 2, GT, C])
        z = sb("z", [P, GT, C])
        ps_T = ps("ps_T", [P, KC, GW])
        ps_h = ps("ps_h", [P, 2, KC, GW])
        ps_y = ps("ps_y", [P, GT, C])
        ln_in = group_norm(sb, sem, "ln_in", EPS, const)
        ln_out = group_norm(sb, sem, "ln_out", EPS, const)
        m = {n: sem(n) for n in ("w_loaded", "w_rest_loaded", "normed", "x_turned", "xT_ready", "routed", "logits_out",
                                   "topped", "r_grown", "router_step", "comb_ready", "h_done", "h_ready",
                                   "gated_ready", "y_done", "y_read", "y_normed", "x_added")}
        eye = const["eye"]
        NX = NE + 1

        with nc.Block() as blk:
            @blk.sync
            def _(sp):
                def load(dst, src, loaded="w_rest_loaded"):
                    sp.dma_start(dst, src).then_inc(m[loaded], 16)

                load(w_r[:], router.rearrange("(k p) n -> p k n", p=P), "w_loaded")
                for e in range(NE):
                    loaded = "w_loaded" if e < 2 else "w_rest_loaded"
                    load(w_1[:, e], w1[e].rearrange("(k p) n -> p k n", p=P), loaded)
                    load(w_2[:, e], w2[e].rearrange("(k p) n -> p k n", p=P), loaded)
                load(w_s[:], s_up.rearrange("(k p) n -> p k n", p=P))
                load(w_2[:, NE], s_down.rearrange("(k p) n -> p k n", p=P))

            @blk.gpsimd
            def _(pool):
                norm_power(ln_in, pool, 0)

                def finish(g):
                    norm_power(ln_out, pool, g)
                    pool.wait_ge(m["y_normed"], g + 1)
                    xs = x_sb[:].rearrange("p (g i) c -> p g i c", i=GT)[:, g]
                    pool.tensor_tensor(xs, xs, z[:], ALU.add).then_inc(m["x_added"], 1)

                def step(g, b, first, last):
                    if not first:
                        finish(g - 1)
                    if not last:
                        norm_power(ln_in, pool, g + 1)

                pool.sem_inc(m["x_added"], 1)
                run_steps(pool, GROUPS, step)
                finish(GROUPS - 1)

            @blk.vector
            def _(dve):
                def inputs(g):
                    norm_measure(ln_in, dve, lambda i: x_sb[:, g * GT + i, :], g)

                def norm(g):
                    norm_apply(ln_in, dve, lambda i: x_norm[:, i, :], lambda i: x_sb[:, g * GT + i, :], g, m["normed"])

                def route(g, b):
                    n = [0]
                    STEPS = 11

                    def link(ins):
                        n[0] += 1
                        ins.then_inc(m["router_step"], 1)
                        dve.wait_ge(m["router_step"], g * STEPS + n[0])

                    dve.wait_ge(m["routed"], g + 1)
                    link(dve.tensor_copy(logits[:], ps_T[:, 0, 0:GT * NC_R].rearrange("p (i e) -> p i e", e=NC_R)))
                    link(dve.tensor_reduce(top[:], logits[:, :, 0:NE], AX, ALU.max))
                    link(dve.tensor_tensor(logits[:, :, 0:NE], logits[:, :, 0:NE],
                                           top[:].unsqueeze(2).broadcast_to([P, GT, NE]), ALU.subtract))
                    dve.tensor_scalar(logits[:, :, NE], logits[:, :, NE], -1.0, None,
                                      ALU.mult).then_inc(m["logits_out"], 1)
                    dve.wait_ge(m["r_grown"], g + 1)
                    link(dve.tensor_reduce(total[:], grown[:, :, 0:NE], AX, ALU.add))
                    link(dve.reciprocal(total[:], total[:]))
                    link(dve.tensor_tensor(probs[:], grown[:, :, 0:NE],
                                           total[:].unsqueeze(2).broadcast_to([P, GT, NE]), ALU.mult))
                    other = probs[:].unsqueeze(2).broadcast_to([P, GT, NE, NE])
                    own = probs[:].unsqueeze(3).broadcast_to([P, GT, NE, NE])
                    link(dve.tensor_tensor(above[:], other, own, ALU.is_gt))
                    link(dve.tensor_tensor(level[:], other, own, ALU.is_equal))
                    before = const["before"].rearrange("p (a b) -> p a b", b=NE).unsqueeze(1)
                    link(dve.tensor_tensor(level[:], level[:], before.broadcast_to([P, GT, NE, NE]), ALU.mult))
                    link(dve.tensor_tensor(above[:], above[:], level[:], ALU.add))
                    link(dve.tensor_reduce(rank[:], above[:], AX, ALU.add))
                    dve.tensor_scalar(top[:], grown[:, :, NE], 1.0, None, ALU.add).then_inc(m["topped"], 1)
                    dve.scalar_tensor_tensor(comb[:, b, :, 0:NE], rank[:], 1.5, probs[:], ALU.is_lt, ALU.mult)
                    dve.wait_ge(m["topped"], g + 1)
                    dve.reciprocal(comb[:, b, :, NE], top[:]).then_inc(m["comb_ready"], 1)
                    assert n[0] == STEPS

                def measured(g, b):
                    norm_measure(ln_out, dve, lambda i: acc[:, b, i, :], g)

                def normed(g, b):
                    dve.wait_ge(m["x_added"], g + 1)
                    norm_apply(ln_out, dve, lambda i: z[:, i, :], lambda i: acc[:, b, i, :], g, m["y_normed"])

                def step(g, b, first, last):
                    for e in range(NX):
                        if e == NE:
                            for k in range(KC):
                                dve.wait_ge(m["gated_ready"], KC * g + k + 1)
                                up = dve.tensor_tensor(hT[:, e % 2, k, :], ps_h[:, 1 - e % 2, k, :], gated[:, k, :],
                                                       ALU.mult)
                            up.then_inc(m["h_ready"], 1)
                        dve.wait_ge(m["y_done"], g * NX + e + 1)
                        if e == 0:
                            dve.wait_ge(m["comb_ready"], g + 1)
                        for i in range(GT):
                            w = comb[:, b, i, e:e + 1]
                            if e == 0:
                                mm = dve.tensor_scalar(acc[:, b, i, :], ps_y[:, i, :], w, None, ALU.mult)
                            else:
                                mm = dve.scalar_tensor_tensor(acc[:, b, i, :], ps_y[:, i, :], w, acc[:, b, i, :],
                                                              ALU.mult, ALU.add)
                        mm.then_inc(m["y_read"], 1)
                        dve.wait_ge(m["y_read"], g * NX + e + 1)
                        if not first:
                            if e == 0:
                                measured(g - 1, 1 - b)
                            if e == 1:
                                normed(g - 1, 1 - b)
                        if not last:
                            if e == 2:
                                inputs(g + 1)
                            if e == 3:
                                norm(g + 1)
                            if e == 6:
                                route(g + 1, 1 - b)

                inputs(0)
                norm(0)
                route(0, 0)
                run_steps(dve, GROUPS, step)
                measured(GROUPS - 1, (GROUPS - 1) % 2)
                normed(GROUPS - 1, (GROUPS - 1) % 2)

            @blk.scalar
            def _(act):
                def turned(g, b):
                    act.wait_ge(m["x_turned"], g + 1)
                    for k in range(KC):
                        last = act.copy(xT[:, b, k, :], ps_T[:, k, :])
                    last.then_inc(m["xT_ready"], 1)

                def routes(g):
                    act.wait_ge(m["logits_out"], g + 1)
                    act.activation(grown[:], logits[:], ACT.Exp).then_inc(m["r_grown"], 1)

                def step(g, b, first, last):
                    for e in range(NX):
                        act.wait_ge(m["h_done"], g * NX + e + 1)
                        if e < NE:
                            if not (first and e < 2):
                                act.wait_ge(m["y_done"], g * NX + max(e - 1, 0))
                            for k in range(KC):
                                mm = act.activation(hT[:, e % 2, k, :], ps_h[:, e % 2, k, :], ACT.Silu)
                            mm.then_inc(m["h_ready"], 1)
                        else:
                            for k in range(KC):
                                act.activation(gated[:, k, :], ps_h[:, e % 2, k, :],
                                               ACT.Silu).then_inc(m["gated_ready"], 1)
                        if not last:
                            if e == 5:
                                turned(g + 1, 1 - b)
                            if e == 7:
                                routes(g + 1)

                turned(0, 0)
                routes(0)
                run_steps(act, GROUPS, step)

            @blk.tensor
            def _(pe):
                def turn(g):
                    pe.wait_ge(m["normed"], g + 1)
                    for k in range(KC):
                        for i in range(GT):
                            last = pe.transpose(ps_T[:, k, i * P:(i + 1) * P], x_norm[:, i, k * P:(k + 1) * P], eye)
                    last.then_inc(m["x_turned"], 1)

                def route(g, b):
                    pe.wait_ge(m["xT_ready"], g + 1)
                    for i in range(GT):
                        for k in range(KC):
                            mm = pe.matmul(ps_T[:, 0, i * NC_R:(i + 1) * NC_R], xT[:, b, k, i * P:(i + 1) * P],
                                           w_r[:, k, :], start=(k == 0), stop=(k == KC - 1))
                    mm.then_inc(m["routed"], 1)

                def hidden(g, e, b, first):
                    if e == 0 and not first:
                        pe.wait_ge(m["gated_ready"], g * KC)
                    elif not (first and e < 2):
                        pe.wait_ge(m["h_ready"], g * NX + max(e - 1, 0))
                    for k2 in range(KC):
                        for k in range(KC):
                            w = w_1[:, e, k, k2 * P:(k2 + 1) * P] if e < NE else w_s[:, k, k2 * P:(k2 + 1) * P]
                            mm = pe.matmul(ps_h[:, e % 2, k2, :], w, xT[:, b, k, :], start=(k == 0),
                                           stop=(k == KC - 1))
                    if e == NE:
                        pe.wait_ge(m["h_ready"], g * NX + NE)
                        for k2 in range(KC):
                            for k in range(KC):
                                mm = pe.matmul(ps_h[:, 1 - e % 2, k2, :], w_s[:, k, C + k2 * P:C + (k2 + 1) * P],
                                               xT[:, b, k, :], start=(k == 0), stop=(k == KC - 1))
                    mm.then_inc(m["h_done"], 1)

                def outputs(g, e):
                    pe.wait_ge(m["h_ready"], g * NX + e + 1)
                    if not (isinstance(g, int) and g == 0 and e == 0):
                        pe.wait_ge(m["y_read"], g * NX + e)
                    for i in range(GT):
                        for k in range(KC):
                            mm = pe.matmul(ps_y[:, i, :], hT[:, e % 2, k, i * P:(i + 1) * P], w_2[:, e, k, :],
                                           start=(k == 0), stop=(k == KC - 1))
                    mm.then_inc(m["y_done"], 1)

                def step(g, b, first, last):
                    for e in range(NX):
                        if first and e == 2:
                            pe.wait_ge(m["w_rest_loaded"], 16 * (2 * NE - 2))
                        hidden(g, e, b, first)
                        if e == 0:
                            if not first:
                                outputs(g - 1, NE)
                        else:
                            outputs(g, e - 1)
                        if e == 5 and not last:
                            turn(g + 1)
                        if e == 6 and not last:
                            route(g + 1, 1 - b)
                    if last:
                        outputs(g, NE)

                turn(0)
                pe.wait_ge(m["w_loaded"], 16 * 5)
                route(0, 0)
                run_steps(pe, GROUPS, step)


def store_layer(nc, x_sb, out):
    with ExitStack() as ctx:
        stored = ctx.enter_context(nc.semaphore("stored"))
        with nc.Block() as blk:
            @blk.sync
            def _(sp):
                for b in range(BATCH):
                    sp.dma_start(out[b].rearrange("(t p) c -> p t c", p=P),
                                 x_sb[:, b * TPB:(b + 1) * TPB, :]).then_inc(stored, 16)
                sp.wait_ge(stored, 16 * BATCH)


def build(nc, io, out, spans, n_const):
    with ExitStack() as ctx:
        x_sb = ctx.enter_context(nc.sbuf_tensor("x_sb", [P, TILES, C], F32))
        c_sb = ctx.enter_context(nc.sbuf_tensor("const", [P, n_const], F32))
        parts = nc.dram_tensor("qk_parts", [3 * 2 * OCT, P, BATCH * SEQ], BF16, kind="Internal").ap()
        x_rest = nc.dram_tensor("x_rest", [P, TILES, C], F32, kind="Internal").ap()
        const = {k: c_sb[:, a:b] for k, (a, b) in spans.items()}
        const["all"], const["dram"] = c_sb[:], io["const"]
        const["passed"] = ctx.enter_context(nc.semaphore("passed"))
        linear_attention_layer(nc, x_sb, const, io["L0_attn_Wq"], io["L0_attn_Wk"], io["L0_attn_Wv"],
                               io["L0_attn_Wo"], io["L0_attn_bo"], io["L0_attn_x"])
        gated_ffn_layer(nc, x_sb, const, io["L0_ffn_w_gate"], io["L0_ffn_w_up"], io["L0_ffn_w_down"])
        with ExitStack() as mid:
            a_sb = mid.enter_context(nc.sbuf_tensor("a_sb", [P, TPB, BATCH, C], F32))
            qk_own = mid.enter_context(nc.sbuf_tensor("qk_own", [P, TPB, BATCH, NH], F32))
            rotary_projection(nc, x_sb, x_rest, const, io["L1_attn_Wqkv"], io["L1_attn_bqkv"], parts, a_sb, qk_own)
            nc.disable_value_cache = True
            softmax_and_solve(nc, x_sb, const, parts, a_sb, qk_own)
            output_projection(nc, x_sb, x_rest, const, io["L1_attn_Wd"], io["L1_attn_bd"], a_sb)
        moe_layer(nc, x_sb, const, io["router"], io["L1_ffn_w1"], io["L1_ffn_w2"],
                  io["L1_ffn_shared_gate_up"], io["L1_ffn_shared_down"])
        store_layer(nc, x_sb, out)


_TURNED = ["L0_attn_Wq", "L0_attn_Wk", "L0_attn_Wv", "L0_attn_Wo", "L0_ffn_w_gate", "L0_ffn_w_up", "L0_ffn_w_down",
           "L1_attn_Wqkv", "L1_attn_Wd"]
_ROWS = ["L0_attn_bo", "L1_attn_bqkv", "L1_attn_bd"]


def kernel(**inputs):
    import concourse.bacc as bacc
    from concourse.bass_utils import run_bass_kernel_spmd

    nc = bacc.Bacc("TRN2", target_bir_lowering=False, num_devices=1)
    arrays, io = {}, {}
    laid = {}
    for name, a in inputs.items():
        a = np.asarray(a)
        if name in _TURNED:
            a = a.T
        if name in _ROWS:
            a = np.broadcast_to(a[None, :], (P, a.shape[0]))
        laid[name] = np.ascontiguousarray(a)
    laid["router"] = np.concatenate([laid.pop("L1_ffn_router_w"), laid.pop("L1_ffn_shared_gate_w")], 1)
    laid["const"], spans = constants_of_shapes()
    for name, a in laid.items():
        arrays[f"in_{name}"] = a
        io[name] = nc.dram_tensor(f"in_{name}", a.shape, mybir.dt.from_np(a.dtype), kind="ExternalInput").ap()
    shape = inputs["L0_attn_x"].shape
    out = nc.dram_tensor("out_x", shape, F32, kind="ExternalOutput").ap()
    build(nc, io, out, spans, laid["const"].shape[1])
    r = run_bass_kernel_spmd(nc, [arrays], core_ids=[0])
    return r.results[0]["out_x"]
```
